# Optimizing a Trainium2 kernel written in Bass

```python
import numpy as np
import jax
import jax.numpy as jnp

def _softmax(x, axis=-1):
    return jax.nn.softmax(x, axis=axis)

def _gelu(x):
    return jax.nn.gelu(x, approximate=True)

def _silu(x):
    return jax.nn.silu(x)

def _sigmoid(x):
    return jax.nn.sigmoid(x)

def _layernorm(x, axis=-1, eps=1e-05):
    m = jnp.mean(x, axis=axis, keepdims=True)
    v = jnp.var(x, axis=axis, keepdims=True)
    return (x - m) / jnp.sqrt(v + eps)

def _scatter_add(tgt, idx, src, axis=0):
    return tgt.at[idx].add(src)

def _segment_sum(src, seg, n):
    return jax.ops.segment_sum(src, seg, n)
kernel_name = 'mk_decoder_preln_d1_seqx_r4_11f102'

def setup_inputs(seed: int=0):
    np.random.seed(seed)
    _w = jnp.asarray

    def _rec_inputs():
        import jax
        import jax.numpy as jnp
        _rk = jax.random.key(seed)
        x = -0.000125 + 0.9999 * jax.random.normal(jax.random.fold_in(_rk, 1), (32, 256, 256), jnp.float32)
        _lenS = 256 - jax.random.randint(jax.random.fold_in(_rk, 7), (32,), 0, max(1, 256 // 4) + 1, jnp.int32)
        _lenS2 = 256 - jax.random.randint(jax.random.fold_in(_rk, 8), (32,), 0, max(1, 256 // 4) + 1, jnp.int32)
        _ctx_1024P = jax.random.normal(jax.random.fold_in(_rk, 11), (32, 16, 256), jnp.float32)
        _ctx_1024c = jax.random.dirichlet(jax.random.fold_in(_rk, 511), 0.3 * jnp.ones((16,), jnp.float32), (32, 256))
        _ctx_1024t = jnp.einsum('bsk,bkd->bsd', _ctx_1024c, _ctx_1024P)
        _ctx_1024t = _ctx_1024t * jax.lax.rsqrt(jnp.mean(jnp.square(_ctx_1024t)) + 1e-12) * 0.953939
        ctx_1024 = -1.52775e-05 + 0.999936 * (_ctx_1024t + 0.3 * jax.random.normal(jax.random.fold_in(_rk, 611), (32, 256, 256), jnp.float32))
        return (x, ctx_1024)
    x, ctx_1024 = _rec_inputs()

    def _L0_attn_setup():
        import jax, jax.numpy as jnp
        import numpy as np
        import math
        B, T, C = (8, 512, 256)
        DIM_ATT, DIM_FFN = (256, 1024)
        N_LAYER, LAYER_ID = (12, 1)
        EPS = 1e-05

        def layer_norm(x, w, b):
            mu = jnp.mean(x, axis=-1, keepdims=True)
            var = jnp.mean(jnp.square(x - mu), axis=-1, keepdims=True)
            return (x - mu) * jax.lax.rsqrt(var + EPS) * w + b

        def time_shift(x):
            return jnp.pad(x, ((0, 0), (1, 0), (0, 0)))[:, :-1, :]

        def wkv(time_decay, time_first, k, v):
            w = -jnp.exp(time_decay)
            u = time_first

            def step(carry, kv_t):
                aa, bb, pp = carry
                kt, vt = kv_t
                ww = u + kt
                qq = jnp.maximum(pp, ww)
                e1 = jnp.exp(pp - qq)
                e2 = jnp.exp(ww - qq)
                y = (e1 * aa + e2 * vt) / (e1 * bb + e2)
                ww2 = pp + w
                qq2 = jnp.maximum(ww2, kt)
                e1b = jnp.exp(ww2 - qq2)
                e2b = jnp.exp(kt - qq2)
                return ((e1b * aa + e2b * vt, e1b * bb + e2b, qq2), y)
            init = (jnp.zeros_like(k[:, 0]), jnp.zeros_like(k[:, 0]), jnp.full_like(k[:, 0], -1e+38))
            kT = jnp.swapaxes(k, 0, 1)
            vT = jnp.swapaxes(v, 0, 1)
            _, yT = jax.lax.scan(step, init, (kT, vT))
            return jnp.swapaxes(yT, 0, 1)
        key = jax.random.key(seed)
        ks = jax.random.split(key, 16)
        r01 = LAYER_ID / (N_LAYER - 1)
        r1a0 = 1.0 - LAYER_ID / N_LAYER
        ddd = (np.arange(C, dtype=np.float32) / C)[None, None, :]
        decay_speed = -5.0 + 8.0 * (np.arange(DIM_ATT, dtype=np.float32) / (DIM_ATT - 1)) ** (0.7 + 1.3 * r01)
        zigzag = np.array([(i + 1) % 3 - 1 for i in range(DIM_ATT)], dtype=np.float32) * 0.5

        def lin(k, out_d, in_d):
            return jax.random.normal(k, (out_d, in_d), jnp.float32) * (1.0 / math.sqrt(in_d))
        return {'x': jax.random.normal(ks[0], (B, T, C), jnp.float32), 'ln1_w': jnp.ones((C,), jnp.float32), 'ln1_b': jnp.zeros((C,), jnp.float32), 'ln2_w': jnp.ones((C,), jnp.float32), 'ln2_b': jnp.zeros((C,), jnp.float32), 'att_tmk': jnp.asarray(ddd ** r1a0), 'att_tmv': jnp.asarray(ddd ** r1a0 + 0.3 * r01), 'att_tmr': jnp.asarray(ddd ** (0.5 * r1a0)), 'time_decay': jnp.asarray(decay_speed), 'time_first': jnp.asarray(np.full(DIM_ATT, math.log(0.3), np.float32) + zigzag), 'Wk': lin(ks[1], DIM_ATT, C), 'Wv': lin(ks[2], DIM_ATT, C), 'Wr': lin(ks[3], DIM_ATT, C), 'Wo': lin(ks[4], C, DIM_ATT), 'ffn_tmk': jnp.asarray(ddd ** r1a0), 'ffn_tmr': jnp.asarray(ddd ** r1a0), 'Wkey': lin(ks[5], DIM_FFN, C), 'Wrec': lin(ks[6], C, C), 'Wval': lin(ks[7], C, DIM_FFN)}
    _L0_attn_all = _L0_attn_setup()
    _L0_attn_in = {k: v for k, v in _L0_attn_all.items() if k in ('ln1_w', 'ln1_b', 'ln2_w', 'ln2_b', 'att_tmk', 'att_tmv', 'att_tmr', 'time_decay', 'time_first', 'Wk', 'Wv', 'Wr', 'Wo', 'ffn_tmk', 'ffn_tmr', 'Wkey', 'Wrec', 'Wval')}
    del _L0_attn_all

    def _L0_xattn_setup():
        import jax, jax.numpy as jnp
        import numpy as np
        import math
        NHEADS = 16
        CAUSAL = True
        NEG_INF = -1e+18
        key = jax.random.key(seed)
        kq, kk, kv = jax.random.split(key, 3)
        B, S, D = (4, 2048, 256)
        q = jax.random.normal(kq, (B, S, D), dtype=jnp.float32)
        k = jax.random.normal(kk, (B, S, D), dtype=jnp.float32)
        v = jax.random.normal(kv, (B, S, D), dtype=jnp.float32)
        return {'q': q, 'k': k, 'v': v}
    _L0_xattn_all = _L0_xattn_setup()
    _L0_xattn_in = {k: v for k, v in _L0_xattn_all.items() if k in ()}
    del _L0_xattn_all

    def _L0_ffn_setup():
        import jax, jax.numpy as jnp
        import numpy as np
        D_MODEL, D_FF, RANK = (256, 1024, 64)
        B, S = (4, 1024)
        key = jax.random.key(seed)
        ks = jax.random.split(key, 7)
        return {'x': jax.random.normal(ks[0], (B, S, D_MODEL), dtype=jnp.float32), 'U1': jax.random.normal(ks[1], (D_MODEL, RANK), dtype=jnp.float32) * 0.02, 'V1': jax.random.normal(ks[2], (RANK, D_FF), dtype=jnp.float32) * 0.02, 'b1': jnp.zeros((D_FF,), dtype=jnp.float32), 'U2': jax.random.normal(ks[3], (D_FF, RANK), dtype=jnp.float32) * 0.02, 'V2': jax.random.normal(ks[4], (RANK, D_MODEL), dtype=jnp.float32) * 0.02, 'b2': jnp.zeros((D_MODEL,), dtype=jnp.float32)}
    _L0_ffn_all = _L0_ffn_setup()
    _L0_ffn_in = {k: v for k, v in _L0_ffn_all.items() if k in ('U1', 'V1', 'b1', 'U2', 'V2', 'b2')}
    del _L0_ffn_all
    return {'x': x, 'ctx_1024': ctx_1024, 'L0_attn_ln1_w': _L0_attn_in['ln1_w'], 'L0_attn_ln1_b': _L0_attn_in['ln1_b'], 'L0_attn_ln2_w': _L0_attn_in['ln2_w'], 'L0_attn_ln2_b': _L0_attn_in['ln2_b'], 'L0_attn_att_tmk': _L0_attn_in['att_tmk'], 'L0_attn_att_tmv': _L0_attn_in['att_tmv'], 'L0_attn_att_tmr': _L0_attn_in['att_tmr'], 'L0_attn_time_decay': _L0_attn_in['time_decay'], 'L0_attn_time_first': _L0_attn_in['time_first'], 'L0_attn_Wk': _L0_attn_in['Wk'], 'L0_attn_Wv': _L0_attn_in['Wv'], 'L0_attn_Wr': _L0_attn_in['Wr'], 'L0_attn_Wo': _L0_attn_in['Wo'], 'L0_attn_ffn_tmk': _L0_attn_in['ffn_tmk'], 'L0_attn_ffn_tmr': _L0_attn_in['ffn_tmr'], 'L0_attn_Wkey': _L0_attn_in['Wkey'], 'L0_attn_Wrec': _L0_attn_in['Wrec'], 'L0_attn_Wval': _L0_attn_in['Wval'], 'L0_ffn_U1': _L0_ffn_in['U1'], 'L0_ffn_V1': _L0_ffn_in['V1'], 'L0_ffn_b1': _L0_ffn_in['b1'], 'L0_ffn_U2': _L0_ffn_in['U2'], 'L0_ffn_V2': _L0_ffn_in['V2'], 'L0_ffn_b2': _L0_ffn_in['b2']}

def reference(x, ctx_1024, L0_attn_ln1_w, L0_attn_ln1_b, L0_attn_ln2_w, L0_attn_ln2_b, L0_attn_att_tmk, L0_attn_att_tmv, L0_attn_att_tmr, L0_attn_time_decay, L0_attn_time_first, L0_attn_Wk, L0_attn_Wv, L0_attn_Wr, L0_attn_Wo, L0_attn_ffn_tmk, L0_attn_ffn_tmr, L0_attn_Wkey, L0_attn_Wrec, L0_attn_Wval, L0_ffn_U1, L0_ffn_V1, L0_ffn_b1, L0_ffn_U2, L0_ffn_V2, L0_ffn_b2):
    import jax
    import jax.numpy as jnp

    def _L0_attn_ref(x, ln1_w, ln1_b, ln2_w, ln2_b, att_tmk, att_tmv, att_tmr, time_decay, time_first, Wk, Wv, Wr, Wo, ffn_tmk, ffn_tmr, Wkey, Wrec, Wval):
        import jax, jax.numpy as jnp
        import numpy as np
        import math
        B, T, C = (8, 512, 256)
        DIM_ATT, DIM_FFN = (256, 1024)
        N_LAYER, LAYER_ID = (12, 1)
        EPS = 1e-05

        def layer_norm(x, w, b):
            mu = jnp.mean(x, axis=-1, keepdims=True)
            var = jnp.mean(jnp.square(x - mu), axis=-1, keepdims=True)
            return (x - mu) * jax.lax.rsqrt(var + EPS) * w + b

        def time_shift(x):
            return jnp.pad(x, ((0, 0), (1, 0), (0, 0)))[:, :-1, :]

        def wkv(time_decay, time_first, k, v):
            w = -jnp.exp(time_decay)
            u = time_first

            def step(carry, kv_t):
                aa, bb, pp = carry
                kt, vt = kv_t
                ww = u + kt
                qq = jnp.maximum(pp, ww)
                e1 = jnp.exp(pp - qq)
                e2 = jnp.exp(ww - qq)
                y = (e1 * aa + e2 * vt) / (e1 * bb + e2)
                ww2 = pp + w
                qq2 = jnp.maximum(ww2, kt)
                e1b = jnp.exp(ww2 - qq2)
                e2b = jnp.exp(kt - qq2)
                return ((e1b * aa + e2b * vt, e1b * bb + e2b, qq2), y)
            init = (jnp.zeros_like(k[:, 0]), jnp.zeros_like(k[:, 0]), jnp.full_like(k[:, 0], -1e+38))
            kT = jnp.swapaxes(k, 0, 1)
            vT = jnp.swapaxes(v, 0, 1)
            _, yT = jax.lax.scan(step, init, (kT, vT))
            return jnp.swapaxes(yT, 0, 1)
        h = layer_norm(x, ln1_w, ln1_b)
        hh = time_shift(h)
        xk = h * att_tmk + hh * (1 - att_tmk)
        xv = h * att_tmv + hh * (1 - att_tmv)
        xr = h * att_tmr + hh * (1 - att_tmr)
        k = xk @ Wk.T
        v = xv @ Wv.T
        sr = jax.nn.sigmoid(xr @ Wr.T)
        rwkv = sr * wkv(time_decay, time_first, k, v)
        x = x + rwkv @ Wo.T
        h = layer_norm(x, ln2_w, ln2_b)
        hh = time_shift(h)
        xk = h * ffn_tmk + hh * (1 - ffn_tmk)
        xr = h * ffn_tmr + hh * (1 - ffn_tmr)
        kk = jnp.square(jax.nn.relu(xk @ Wkey.T))
        kv = kk @ Wval.T
        x = x + jax.nn.sigmoid(xr @ Wrec.T) * kv
        return x

    def _L0_xattn_ref(q, k, v):
        import jax, jax.numpy as jnp
        import numpy as np
        import math
        NHEADS = 16
        CAUSAL = True
        NEG_INF = -1e+18
        B, S, D = q.shape
        hd = D // NHEADS
        qh = q.reshape(B, S, NHEADS, hd)
        kh = k.reshape(B, S, NHEADS, hd)
        vh = v.reshape(B, S, NHEADS, hd)
        scores = jnp.einsum('bsqd,bskd->bsqk', qh, kh) / math.sqrt(hd)
        if CAUSAL:
            mask = jnp.tril(jnp.ones((NHEADS, NHEADS), dtype=bool))
            scores = jnp.where(mask, scores, jnp.asarray(NEG_INF, scores.dtype))
        attn = jax.nn.softmax(scores, axis=-1)
        out = jnp.einsum('bsqk,bskd->bsqd', attn, vh)
        return out.reshape(B, S, D)

    def _L0_ffn_ref(x, U1, V1, b1, U2, V2, b2):
        import jax, jax.numpy as jnp
        import numpy as np
        D_MODEL, D_FF, RANK = (256, 1024, 64)
        B, S = (4, 1024)
        P = jnp.einsum('bsd,dr->bsr', x, U1)
        H = jax.nn.gelu(jnp.einsum('bsr,rf->bsf', P, V1) + b1)
        Q = jnp.einsum('bsf,fr->bsr', H, U2)
        return jnp.einsum('bsr,rd->bsd', Q, V2) + b2
    x = x + _L0_attn_ref(_layernorm(x, axis=-1), L0_attn_ln1_w, L0_attn_ln1_b, L0_attn_ln2_w, L0_attn_ln2_b, L0_attn_att_tmk, L0_attn_att_tmv, L0_attn_att_tmr, L0_attn_time_decay, L0_attn_time_first, L0_attn_Wk, L0_attn_Wv, L0_attn_Wr, L0_attn_Wo, L0_attn_ffn_tmk, L0_attn_ffn_tmr, L0_attn_Wkey, L0_attn_Wrec, L0_attn_Wval)
    x = x + _L0_xattn_ref(_layernorm(x, axis=-1), ctx_1024, ctx_1024)
    x = x + _L0_ffn_ref(_layernorm(x, axis=-1), L0_ffn_U1, L0_ffn_V1, L0_ffn_b1, L0_ffn_U2, L0_ffn_V2, L0_ffn_b2)
    return x

_drawn_inputs = setup_inputs


def setup_inputs(seed=0):
    import zlib

    import numpy as np

    out = dict(_drawn_inputs(seed))
    spreads = {'L0_attn_ln1_w': (1.0, 0.2),
     'L0_attn_ln1_b': (0.0, 0.315),
     'L0_attn_ln2_w': (1.0, 0.2),
     'L0_attn_ln2_b': (0.0, 0.1),
     'L0_ffn_b1': (0.0, 0.8),
     'L0_ffn_b2': (0.0, 0.8)}
    factors = {'L0_attn_time_first': 95.96,
     'L0_ffn_U1': 8.0,
     'L0_ffn_V1': 8.0,
     'L0_ffn_U2': 8.0,
     'L0_ffn_V2': 8.0}
    for name, (base, spread) in spreads.items():
        noise = np.random.default_rng([zlib.crc32(name.encode()), seed]).standard_normal(out[name].shape)
        drawn = base * np.exp(spread * noise) if base else spread * noise
        out[name] = jnp.asarray(drawn.astype(out[name].dtype))
    for name, factor in factors.items():
        out[name] = (out[name] * factor).astype(out[name].dtype)
    return out
```

```python
from contextlib import ExitStack

import concourse.bass as bass
from concourse import mybir

ALU = mybir.AluOpType
ACT = mybir.ActivationFunctionType
AX = mybir.AxisListType
F32 = mybir.dt.float32

P = 128
C = 256
CH = C // P
T = 256
SEQ = 2
W = SEQ * T
TT = W // P
NH, HD = 16, 16
FF = 1024
FT = FF // P
RANK = 64
EPS = 1e-5
START = -1e38
MASKED = -1e18
EXP_SET = "natural_log_exp_and_others"
GELU_SET = "gelu_apprx_tanh_and_others"
GAP = 43.0
HB = 4
NB = NH // HB

VECS = ["ln1_w", "ln1_b", "ln2_w", "ln2_b", "att_tmk", "att_tmv", "att_tmr", "time_decay",
        "time_first", "ffn_tmk", "ffn_tmr"]
B1_AT = len(VECS) * CH


def score_parts():
    parts, at = [], 0
    for i in range(1, NB):
        parts.append(("rect", i, at))
        at += HB * (HB * i) * HD
    for r in range(HB):
        parts.append(("row", r, at))
        at += NB * (r + 1) * HD
    return parts, at


def value_parts():
    parts, at = [], 0
    for i in range(NB):
        keys = HB * (i + 1)
        parts.append((i, keys, at))
        at += HB * HD * keys
    return parts, at


def build(nc, x, ctx, vecs, b2, wk, wv, wr, wo, wkey, wrec, wval, u1, v1, u2, v2, out):
    NG = x.shape[0] // SEQ
    REST_W = 16 * 12
    LAST = NG + 3
    LOOP = (3, NG - 1)
    assert (LOOP[1] - LOOP[0]) % 2 == 0
    S_PARTS, S_SIZE = score_parts()
    V_PARTS, V_SIZE = value_parts()

    with ExitStack() as stack:
        def sb(name, shape):
            return stack.enter_context(nc.sbuf_tensor(name, shape, F32))

        def sem(name):
            return stack.enter_context(nc.semaphore(name))

        vec = sb("vec", [P, B1_AT + FT])
        b2_row = sb("b2_row", [P, C])
        w_k, w_v, w_r, w_o, w_rec = (sb(n, [P, CH, C]) for n in ("w_k", "w_v", "w_r", "w_o", "w_rec"))
        w_key = sb("w_key", [P, CH, FF])
        w_val = sb("w_val", [P, FT, C])
        w_u1 = sb("w_u1", [P, CH, 2 * RANK])
        w_v1 = sb("w_v1", [P, FT // 2, P])
        w_u2 = sb("w_u2", [P, FT, RANK])
        w_v2 = sb("w_v2", [P, C])
        ident = sb("ident", [P, P])
        decay = sb("decay", [P, CH])
        decay_row = sb("decay_row", [P, CH, T])
        eps_col = sb("eps_col", [P, 1])
        nln2_col = sb("nln2_col", [P, 1])

        def col(name, f):
            at = VECS.index(name) * CH + f
            return vec[:, at:at + 1]

        x_in = sb("x_in", [P, TT, C])
        n1 = [sb(f"n1_{p}", [P, TT, C]) for p in range(2)]
        h = sb("h", [P, CH * SEQ, T + 1])
        diff = sb("diff", [P, CH, W])
        xk, xv, xr = (sb(n, [P, CH, W]) for n in ("xk", "xv", "xr"))
        kT, vT, gate_r = (sb(n, [P, CH, W]) for n in ("kT", "vT", "gate_r"))
        pp, aa, bb = (sb(n, [P, CH * SEQ, T + 1]) for n in ("pp", "aa", "bb"))
        e1, rr = (sb(n, [P, CH, W]) for n in ("e1", "rr"))
        e2 = kT
        num = sb("num", [P, CH, W])
        x1 = sb("x1", [P, TT, C])
        n2 = sb("n2", [P, TT, C])
        gate_rec = sb("gate_rec", [P, TT, C])
        hidden = sb("hidden", [P, FT, W])
        x2 = [sb(f"x2_{p}", [P, TT, C]) for p in range(2)]
        q = sb("q", [P, TT, C])
        kv_ctx = [sb(f"kv_ctx{p}", [P, TT, C]) for p in range(2)]
        prod = [sb(f"prod{s}", [P, max(S_SIZE, V_SIZE)]) for s in range(2)]
        score = sb("score", [P, TT * NH, NH])
        prob = sb("prob", [P, TT * NH, NH])
        top = sb("top", [P, TT * NH])
        mass = sb("mass", [P, TT * NH])
        o_att = sb("o_att", [P, TT * NH, HD])
        x3 = sb("x3", [P, TT, C])
        n4 = sb("n4", [P, TT, C])
        n4T = sb("n4T", [P, CH, W])
        pT = sb("pT", [P, W])
        qT = sb("qT", [P, W])
        y_out = sb("y_out", [P, TT, C])
        stat = {n: sb(f"stat{n}", [P, TT, 6]) for n in (1, 2, 3, 4)}
        mv = {n: sb(f"mv{n}", [P, TT, 2]) for n in (1, 2, 3, 4)}
        lnv = {n: sb(f"lnv{n}", [P, TT]) for n in (1, 2, 3, 4)}
        rstd = {n: sb(f"rstd{n}", [P, TT]) for n in (1, 2, 3, 4)}
        inv1, vx, lnx = (sb(n, [P, TT]) for n in ("inv1", "vx", "lnx"))
        waited = sb("waited", [P, 1])
        back = [sb(f"back{p}", [P, TT]) for p in range(2)]

        bank = [stack.enter_context(nc.psum_tensor(f"bank{n}", [P, 512], F32)) for n in range(8)]
        HIDDEN_BANKS = [2, 3, 0, 1]

        x_again = sem("x_again")
        x_loaded, ctx_loaded, out_stored = sem("x_loaded"), sem("ctx_loaded"), sem("out_stored")
        vec_loaded, att_w_loaded, rest_w_loaded = sem("vec_loaded"), sem("att_w_loaded"), sem("rest_w_loaded")
        ident_done, const_done, decay_exp, decay_done = sem("ident_done"), sem("const_done"), sem("decay_exp"), sem("decay_done")
        stats_read = {n: sem(f"stats_read{n}") for n in (1, 2, 3, 4)}
        mean_var = {n: sem(f"mean_var{n}") for n in (1, 2, 3, 4)}
        vx_done, lnsum_done = sem("vx_done"), sem("lnsum_done")
        n1_done, n2_done, q_done, n4_done = sem("n1_done"), sem("n2_done"), sem("q_done"), sem("n4_done")
        diff1_done, diff2_done = sem("diff1_done"), sem("diff2_done")
        xk_done, xv_done, xr_done = sem("xk_done"), sem("xv_done"), sem("xr_done")
        xk2_done, xr2_done = sem("xk2_done"), sem("xr2_done")
        pp_done, e1_arg, rr_raw, rr_arg = sem("pp_done"), sem("e1_arg"), sem("rr_raw"), sem("rr_arg")
        aa_done, bb_done = sem("aa_done"), sem("bb_done")
        gnum_done, rwkv_done = sem("gnum_done"), sem("rwkv_done")
        x1_done, res_done = sem("x1_done"), sem("res_done")
        gated_done, x2_done = sem("gated_done"), sem("x2_done")
        s_sum, v_sum = sem("s_sum"), sem("v_sum")
        top_done, shift_done, mass_done, inv_done = sem("top_done"), sem("shift_done"), sem("mass_done"), sem("inv_done")
        o_norm, x3_done = sem("o_norm"), sem("x3_done")
        y_done = sem("y_done")
        s_prod, v_prod = sem("s_prod"), sem("v_prod")
        e2_arg, e2v_done, rv_done, num_done, den_done = sem("e2_arg"), sem("e2v_done"), sem("rv_done"), sem("num_done"), sem("den_done")
        x3b_done = sem("x3b_done")
        k_out, v_out, r_gate, rec_gate = sem("k_out"), sem("v_out"), sem("r_gate"), sem("rec_gate")
        e1_exp, e2_exp, rr_exp = sem("e1_exp"), sem("e2_exp"), sem("rr_exp")
        den_ln, den_inv = sem("den_ln"), sem("den_inv")
        h1_done, h2_done, n4T_done = sem("h1_done"), sem("h2_done"), sem("n4T_done")
        ln_done = {n: sem(f"ln_done{n}") for n in (1, 2, 3, 4)}
        rstd_done = {n: sem(f"rstd_done{n}") for n in (1, 2, 3, 4)}
        inv1_done, lnx_done = sem("inv1_done"), sem("lnx_done")
        pT_done, qT_done = sem("pT_done"), sem("qT_done")
        gelu_done, relu_done, square_done = sem("gelu_done"), sem("relu_done"), sem("square_done")
        prob_done = sem("prob_done")
        k_mm, v_mm, r_mm = sem("k_mm"), sem("v_mm"), sem("r_mm")
        wo_mm, rec_mm, val_mm, v2_mm = sem("wo_mm"), sem("rec_mm"), sem("val_mm"), sem("v2_mm")
        tr1_mm, tr2_mm, tr4_mm = sem("tr1_mm"), sem("tr2_mm"), sem("tr4_mm")
        u1_mm, u2_mm = sem("u1_mm"), sem("u2_mm")
        v1_mm, key_mm = sem("v1_mm"), sem("key_mm")

        block = stack.enter_context(nc.Block())

        def upto(g, per, k=None):
            return per * g + (per if k is None else k)

        def some(g):
            return not isinstance(g, int) or g > 0

        def drive(eng, step):
            for i in range(-1, LOOP[0]):
                step(i, i % 2, lambda lag, i=i: 0 <= i - lag < NG)
            with eng.Fori(LOOP[0], LOOP[1] - 1, 2) as i:
                step(i, LOOP[0] % 2, lambda lag: True)
                step(i + 1, (LOOP[0] + 1) % 2, lambda lag: True)
            for i in range(LOOP[1], LAST):
                step(i, i % 2, lambda lag, i=i: 0 <= i - lag < NG)

        def seqs(t, f):
            return t[:, f, :].rearrange("p (s t) -> p s t", s=SEQ)

        def now(t, f):
            return t[:, SEQ * f:SEQ * f + SEQ, 1:T + 1]

        def before(t, f):
            return t[:, SEQ * f:SEQ * f + SEQ, 0:T]

        def pair(t, s):
            return t[:, 2 * s:2 * s + 2, :].rearrange("p t c -> p (t c)")

        x_g = x.rearrange("(g s) (h p) c -> g p (s h) c", s=SEQ, p=P)
        ctx_g = ctx.rearrange("(g s) (h p) c -> g p (s h) c", s=SEQ, p=P)
        out_g = out.rearrange("(g s) (h p) c -> g p (s h) c", s=SEQ, p=P)

        @block.sync
        def _(sp):
            sp.dma_start(vec[:, :], vecs).then_inc(vec_loaded, 16)
            for t, w in ((w_k, wk), (w_v, wv), (w_r, wr)):
                sp.dma_start(t[:, :, :], w.rearrange("(c p) n -> p c n", p=P)).then_inc(att_w_loaded, 16)
            for t, w in ((w_o, wo), (w_rec, wrec), (w_key, wkey), (w_val, wval), (w_u2, u2)):
                sp.dma_start(t[:, :, :], w.rearrange("(c p) n -> p c n", p=P)).then_inc(rest_w_loaded, 16)
            v1_t = v1.rearrange("r (j e n) -> e r j n", e=2, n=P)
            for e in range(2):
                half = slice(RANK * e, RANK * e + RANK)
                sp.dma_start(w_u1[:, :, half], u1.rearrange("(c p) n -> p c n", p=P)).then_inc(rest_w_loaded, 16)
                sp.dma_start(w_v1[half, :, :], v1_t[e]).then_inc(rest_w_loaded, 16)
                sp.dma_start(w_v2[half, :], v2).then_inc(rest_w_loaded, 16)
            sp.dma_start(b2_row[:, :], b2.to_broadcast([P, C])).then_inc(rest_w_loaded, 16)

            def step(i, p, on):
                c, d = i - 2, i - 3
                if on(-1):
                    if some(i + 1):
                        sp.wait_ge(n1_done, upto(i, 1))
                    sp.dma_start(x_in[:, :, :], x_g[i + 1]).then_inc(x_loaded, 16)
                if on(1):
                    if some(i - 1):
                        sp.wait_ge(ctx_loaded, 16 * (i - 1))
                    if some(i - 2):
                        sp.wait_ge(v_prod, upto(i - 3, 4))
                    sp.dma_start(kv_ctx[(p + 1) % 2][:, :, :], ctx_g[i - 1]).then_inc(ctx_loaded, 16)
                    sp.wait_ge(x1_done, upto(i - 1, 2))
                    sp.dma_start(n1[(p + 1) % 2][:, :, :], x_g[i - 1]).then_inc(x_again, 16)
                if on(3):
                    sp.wait_ge(y_done, upto(d, 2))
                    sp.dma_start(out_g[d], y_out[:, :, :]).then_inc(out_stored, 16)

            drive(sp, step)
            sp.wait_ge(out_stored, 16 * NG)

        @block.gpsimd
        def _(pool):
            pool.memset(ident[:, :], 0.0).then_inc(ident_done, 1)
            pool.wait_ge(ident_done, 1)
            pool.affine_select(out=ident[:, :], in_=ident[:, :], compare_op=ALU.not_equal, fill=1.0,
                               base=0, pattern=[[-1, P]], channel_multiplier=1).then_inc(ident_done, 1)
            pool.memset(score[:, :, :], MASKED * float(HD) ** 0.5)
            pool.memset(h[:, :, 0:1], 0.0)
            pool.memset(pp[:, :, 0:1], START)
            pool.memset(aa[:, :, 0:1], 0.0)
            pool.memset(bb[:, :, 0:1], 0.0)
            pool.memset(nln2_col[:, :], -0.6931471805599453)
            pool.memset(eps_col[:, :], EPS).then_inc(const_done, 1)
            pool.wait_ge(const_done, 1)

            def score_products(g, p, t, slot):
                qh = q[:, t, :].rearrange("p (h d) -> p h d", h=NH)
                kh = kv_ctx[p][:, t, :].rearrange("p (h d) -> p h d", h=NH)
                qb = q[:, t, :].rearrange("p (b r d) -> p b r d", b=NB, r=HB)
                kb = kv_ctx[p][:, t, :].rearrange("p (b r d) -> p b r d", b=NB, r=HB)
                for kind, n, at in S_PARTS:
                    if kind == "rect":
                        shape = [P, HB, HB * n, HD]
                        a = qh[:, HB * n:HB * n + HB, :].unsqueeze(2).to_broadcast(shape)
                        b = kh[:, 0:HB * n, :].unsqueeze(1).to_broadcast(shape)
                    else:
                        shape = [P, NB, n + 1, HD]
                        a = qb[:, :, n:n + 1, :].to_broadcast(shape)
                        b = kb[:, :, 0:n + 1, :]
                    o = prod[slot][:, at:at + shape[1] * shape[2] * HD].rearrange(
                        "p (a b d) -> p a b d", a=shape[1], b=shape[2])
                    ins = pool.tensor_tensor(o, a, b, ALU.mult)
                ins.then_inc(s_prod, 1)

            def value_products(g, p, t, slot):
                ph = prob[:, NH * t:NH * t + NH, :]
                vh = kv_ctx[p][:, t, :].rearrange("p (h d) -> p d h", h=NH)
                for n, keys, at in V_PARTS:
                    shape = [P, HB, HD, keys]
                    o = prod[slot][:, at:at + HB * HD * keys].rearrange("p (a d b) -> p a d b", a=HB, d=HD)
                    ins = pool.tensor_tensor(
                        o, ph[:, HB * n:HB * n + HB, 0:keys].unsqueeze(2).to_broadcast(shape),
                        vh[:, :, 0:keys].unsqueeze(1).to_broadcast(shape), ALU.mult)
                ins.then_inc(v_prod, 1)

            def step(i, p, on):
                a, c, d = i, i - 2, i - 3
                if on(3):
                    pool.wait_ge(prob_done, upto(d, 2, 2))
                    pool.wait_ge(v_sum, upto(d, 4, 2))
                    value_products(d, (p + 1) % 2, 3, 0)
                if on(2):
                    pool.wait_ge(ctx_loaded, 16 * (c + 1))
                    pool.wait_ge(q_done, upto(c, 1))
                    if some(c):
                        pool.wait_ge(v_sum, upto(c - 1, 4, 3))
                    score_products(c, p, 0, 1)
                if on(0):
                    for f in range(CH):
                        pool.wait_ge(pp_done, upto(a, 2, f + 1))
                        pool.wait_ge(rr_raw, upto(a, 2, f + 1))
                        pool.tensor_tensor(seqs(e2, f), seqs(kT, f), now(pp, f), ALU.subtract)\
                            .then_inc(e2_arg, 1)
                if on(2):
                    if some(c):
                        pool.wait_ge(v_sum, upto(c - 1, 4, 4))
                    score_products(c, p, 1, 0)
                if on(0):
                    for f in range(CH):
                        pool.wait_ge(e2_exp, upto(a, 2, f + 1))
                        pool.wait_ge(v_out, upto(a, 2, f + 1))
                        if some(a):
                            pool.wait_ge(wo_mm, upto(a - 1, 2))
                        pool.tensor_tensor(num[:, f, :], e2[:, f, :], vT[:, f, :], ALU.mult)\
                            .then_inc(e2v_done, 1)
                if on(3):
                    pool.wait_ge(x3_done, upto(d, 2))
                    pool.wait_ge(rest_w_loaded, REST_W)
                    if some(d):
                        pool.wait_ge(out_stored, 16 * d)
                    pool.tensor_tensor(y_out[:, :, :], x3[:, :, :],
                                       b2_row[:, :].unsqueeze(1).to_broadcast([P, TT, C]), ALU.add)\
                        .then_inc(x3b_done, 1)
                if on(2):
                    pool.wait_ge(s_sum, upto(c, 4, 1))
                    score_products(c, p, 2, 1)
                    pool.wait_ge(s_sum, upto(c, 4, 2))
                    score_products(c, p, 3, 0)
                    pool.wait_ge(prob_done, upto(c, 2, 1))
                    pool.wait_ge(s_sum, upto(c, 4, 3))
                    value_products(c, p, 0, 1)
                if on(0):
                    for f in range(CH):
                        pool.wait_ge(rr_exp, upto(a, 2, f + 1))
                        pool.wait_ge(aa_done, upto(a, 2, f + 1))
                        pool.tensor_tensor(num[:, f, :], rr[:, f, :], vT[:, f, :], ALU.mult)\
                            .then_inc(rv_done, 1)
                    for f in range(CH):
                        pool.wait_ge(bb_done, upto(a, 2, f + 1))
                        pool.wait_ge(rv_done, upto(a, 2, f + 1))
                        pool.tensor_tensor(seqs(rr, f), seqs(rr, f), before(bb, f), ALU.add)\
                            .then_inc(den_done, 1)
                    for f in range(CH):
                        pool.wait_ge(aa_done, upto(a, 2, f + 1))
                        pool.tensor_tensor(seqs(num, f), seqs(num, f), before(aa, f), ALU.add)\
                            .then_inc(num_done, 1)
                if on(2):
                    pool.wait_ge(s_sum, upto(c, 4, 4))
                    value_products(c, p, 1, 0)
                    pool.wait_ge(prob_done, upto(c, 2, 2))
                    pool.wait_ge(v_sum, upto(c, 4, 1))
                    value_products(c, p, 2, 1)

            drive(pool, step)

        @block.scalar
        def _(act):
            act.preload_act_table_set(EXP_SET)
            act.wait_ge(vec_loaded, 16)
            at = VECS.index("time_decay") * CH
            act.activation(decay[:, :], vec[:, at:at + CH], ACT.Exp).then_inc(decay_exp, 1)
            act.wait_ge(const_done, 1)

            def rstd_of(n, g):
                act.wait_ge(mean_var[n], upto(g, 1))
                act.activation(lnv[n][:, :], mv[n][:, :, 1], ACT.Ln, bias=eps_col[:, :])\
                    .then_inc(ln_done[n], 1)
                act.wait_ge(ln_done[n], upto(g, 1))
                act.activation(rstd[n][:, :], lnv[n][:, :], ACT.Exp, scale=-0.5)\
                    .then_inc(rstd_done[n], 1)

            def step(i, p, on):
                a, b, c, d = i, i - 1, i - 2, i - 3
                if on(0):
                    for f in range(CH):
                        act.wait_ge(k_mm, upto(a, 2, f + 1))
                        if some(a):
                            act.wait_ge(aa_done, upto(a - 1, 2))
                        act.activation(kT[:, f, :], bank[f][:, :], ACT.Copy).then_inc(k_out, 1)
                if on(2):
                    rstd_of(3, c)
                if on(0):
                    for f in range(CH):
                        act.wait_ge(v_mm, upto(a, 2, f + 1))
                        if some(a):
                            act.wait_ge(rv_done, upto(a - 1, 2))
                        act.activation(vT[:, f, :], bank[2 + f][:, :], ACT.Copy).then_inc(v_out, 1)
                    for f in range(CH):
                        act.wait_ge(e1_arg, upto(a, 2, f + 1))
                        act.activation(e1[:, f, :], e1[:, f, :], ACT.Exp).then_inc(e1_exp, 1)
                        act.wait_ge(rr_arg, upto(a, 2, f + 1))
                        act.activation(rr[:, f, :], rr[:, f, :], ACT.Exp).then_inc(rr_exp, 1)
                if on(1):
                    rstd_of(2, b)
                if on(0):
                    for f in range(CH):
                        act.wait_ge(e2_arg, upto(a, 2, f + 1))
                        act.activation(e2[:, f, :], e2[:, f, :], ACT.Exp).then_inc(e2_exp, 1)
                if on(3):
                    rstd_of(4, d)
                if on(1):
                    for f in range(CH):
                        act.wait_ge(tr2_mm, upto(b, 2, f + 1))
                        if some(b):
                            act.wait_ge(xk2_done, upto(b - 1, 1))
                        if on(0):
                            act.wait_ge(xr_done, upto(a, 1))
                        act.activation(now(h, f), bank[6 + f][:, :].rearrange("p (s t) -> p s t", s=SEQ),
                                       ACT.Identity, bias=col("ln2_b", f), scale=col("ln2_w", f))\
                            .then_inc(h2_done, 1)
                if on(3):
                    for f in range(CH):
                        act.wait_ge(tr4_mm, upto(d, 2, f + 1))
                        if some(d):
                            act.wait_ge(u1_mm, upto(d - 1, 1))
                        act.activation(n4T[:, f, :], bank[4 + f][:, :], ACT.Copy).then_inc(n4T_done, 1)
                act.preload_act_table_set(GELU_SET)
                if on(0):
                    for f in range(CH):
                        act.wait_ge(r_mm, upto(a, 2, f + 1))
                        if some(a):
                            act.wait_ge(gnum_done, upto(a - 1, 2))
                        act.activation(gate_r[:, f, :], bank[f][:, :], ACT.Tanh, scale=0.5).then_inc(r_gate, 1)
                if on(3):
                    act.wait_ge(u1_mm, upto(d, 1))
                    if some(d):
                        act.wait_ge(v1_mm, upto(d - 1, 8))
                    act.activation(pT[:, :], bank[3][:, :], ACT.Copy).then_inc(pT_done, 1)
                    for j in range(FT):
                        act.wait_ge(v1_mm, upto(d, 8, j + 1))
                        if j == 0 and on(2):
                            act.wait_ge(val_mm, upto(c, 2))
                        act.activation(hidden[:, j, :], bank[HIDDEN_BANKS[j % 4]][:, :], ACT.Gelu_apprx_tanh,
                                       bias=vec[:, B1_AT + j:B1_AT + j + 1]).then_inc(gelu_done, 1)
                    act.wait_ge(u2_mm, upto(d, 1))
                    if some(d):
                        act.wait_ge(v2_mm, upto(d - 1, 2))
                    act.activation(qT[:, :], bank[4][:, :], ACT.Copy).then_inc(qT_done, 1)
                if on(1):
                    for s in range(2):
                        act.wait_ge(rec_mm, upto(b, 2, s + 1))
                        if some(b):
                            act.wait_ge(x2_done, upto(b - 1, 2))
                        act.activation(pair(gate_rec, s), bank[4 + s][:, :], ACT.Tanh, scale=0.5)\
                            .then_inc(rec_gate, 1)
                act.preload_act_table_set(EXP_SET)

                def probabilities(s):
                    rows = slice(2 * NH * s, 2 * NH * s + 2 * NH)
                    act.wait_ge(shift_done, upto(c, 2, s + 1))
                    act.activation(prob[:, rows, :], prob[:, rows, :], ACT.Exp, scale=float(HD) ** -0.5)\
                        .then_inc(prob_done, 1)

                def squared_relu(j):
                    act.wait_ge(key_mm, upto(b, 8, j + 1))
                    if j == 0:
                        if some(b):
                            act.wait_ge(val_mm, upto(b - 1, 2))
                        if on(3):
                            act.wait_ge(u2_mm, upto(d, 1))
                    act.activation(hidden[:, j, :], bank[HIDDEN_BANKS[j % 4]][:, :], ACT.Relu)\
                        .then_inc(relu_done, 1)

                def square(j):
                    act.wait_ge(relu_done, upto(b, 8, j + 1))
                    act.activation(hidden[:, j, :], hidden[:, j, :], ACT.Square).then_inc(square_done, 1)

                if on(2):
                    probabilities(0)
                for j in range(FT):
                    if on(1):
                        squared_relu(j)
                        if j:
                            square(j - 1)
                    if j == 1 and on(-1):
                        act.wait_ge(mean_var[1], upto(a + 1, 1))
                        act.activation(lnv[1][:, :], mv[1][:, :, 1], ACT.Ln, bias=eps_col[:, :])\
                            .then_inc(ln_done[1], 1)
                        act.wait_ge(ln_done[1], upto(a + 1, 1))
                        act.activation(inv1[:, :], lnv[1][:, :], ACT.Exp, scale=-1.0).then_inc(inv1_done, 1)
                    if j == 2 and on(-1):
                        act.wait_ge(vx_done, upto(a + 1, 1))
                        act.activation(lnx[:, :], vx[:, :], ACT.Ln, bias=eps_col[:, :]).then_inc(lnx_done, 1)
                        act.wait_ge(lnx_done, upto(a + 1, 1))
                        act.activation(back[(p + 1) % 2][:, :], lnx[:, :], ACT.Exp, scale=0.5)
                        act.wait_ge(lnsum_done, upto(a + 1, 1))
                        act.activation(rstd[1][:, :], lnv[1][:, :], ACT.Exp, scale=-0.5).then_inc(rstd_done[1], 1)
                    if j == 4 and on(0):
                        for f in range(CH):
                            act.wait_ge(den_done, upto(a, 2, f + 1))
                            act.activation(rr[:, f, :], rr[:, f, :], ACT.Ln).then_inc(den_ln, 1)
                    if j == 5 and on(0):
                        for f in range(CH):
                            act.wait_ge(den_ln, upto(a, 2, f + 1))
                            act.activation(rr[:, f, :], rr[:, f, :], ACT.Exp, scale=-1.0, bias=nln2_col[:, :])\
                                .then_inc(den_inv, 1)
                if on(1):
                    square(FT - 1)
                if on(2):
                    probabilities(1)
                if on(-1):
                    for f in range(CH):
                        act.wait_ge(tr1_mm, upto(a + 1, 2, f + 1))
                        if some(a + 1):
                            act.wait_ge(xr_done, upto(a, 1))
                        if on(1):
                            act.wait_ge(xk2_done, upto(b, 1))
                        act.activation(now(h, f), bank[2 + f][:, :].rearrange("p (s t) -> p s t", s=SEQ),
                                       ACT.Identity, bias=col("ln1_b", f), scale=col("ln1_w", f))\
                            .then_inc(h1_done, 1)

            drive(act, step)

        @block.tensor
        def _(pe):
            pe.wait_ge(ident_done, 2)
            pe.wait_ge(att_w_loaded, 16 * 3)
            pe.wait_ge(rest_w_loaded, REST_W)

            def feature_major(banks, w, src, done):
                for fo in range(CH):
                    for fi in range(CH):
                        mm = pe.matmul(bank[banks[fo]][:, :], w[:, fi, P * fo:P * fo + P], src[:, fi, :],
                                       start=(fi == 0), stop=(fi == CH - 1))
                    mm.then_inc(done, 1)

            def token_major(banks, src, w, done):
                for s in range(2):
                    for t in (2 * s, 2 * s + 1):
                        for fi in range(CH):
                            mm = pe.matmul(bank[banks[s]][:, C * (t % 2):C * (t % 2) + C],
                                           src[:, fi, P * t:P * t + P], w[:, fi, :],
                                           start=(fi == 0), stop=(fi == CH - 1))
                    mm.then_inc(done, 1)

            def transposes(banks, src, done):
                for f in range(CH):
                    for t in range(TT):
                        mm = pe.transpose(bank[banks[f]][:, P * t:P * t + P], src[:, t, P * f:P * f + P],
                                          ident[:, :])
                    mm.then_inc(done, 1)

            def step(i, p, on):
                a, b, c, d = i, i - 1, i - 2, i - 3
                if isinstance(i, int) and i >= LOOP[1]:
                    if 0 <= i - 2 < NG:
                        pe.wait_ge(relu_done, upto(i - 2, 8))
                        pe.wait_ge(rec_gate, upto(i - 2, 2))
                    if 0 <= i - 1 < NG:
                        pe.wait_ge(r_gate, upto(i - 1, 2))
                    pe.wait_ge(y_done, upto(min(i - 4, NG - 1), 2))
                    pe.wait_ge(gated_done, upto(min(i - 3, NG - 1), 2))
                if on(0):
                    pe.wait_ge(xk_done, upto(a, 1))
                    if some(a - 1):
                        pe.wait_ge(relu_done, upto(a - 2, 8))
                    elif some(a):
                        pe.wait_ge(r_gate, upto(a - 1, 2))
                    feature_major((0, 1), w_k, xk, k_mm)
                if on(1):
                    pe.wait_ge(rwkv_done, upto(b, 2))
                    if some(b):
                        pe.wait_ge(gated_done, upto(b - 1, 2))
                    token_major((6, 7), num, w_o, wo_mm)
                if on(0):
                    pe.wait_ge(xv_done, upto(a, 1))
                    pe.wait_ge(h1_done, upto(a, 2))
                    feature_major((2, 3), w_v, xv, v_mm)
                    pe.wait_ge(xr_done, upto(a, 1))
                    pe.wait_ge(k_out, upto(a, 2))
                    feature_major((0, 1), w_r, xr, r_mm)
                if on(1):
                    pe.wait_ge(n2_done, upto(b, 1))
                    pe.wait_ge(x1_done, upto(b, 2))
                    transposes((6, 7), n2, tr2_mm)
                if on(3):
                    pe.wait_ge(n4_done, upto(d, 1))
                    pe.wait_ge(rec_gate, upto(d + 1, 2) if on(2) else upto(d, 2))
                    transposes((4, 5), n4, tr4_mm)
                    pe.wait_ge(n4T_done, upto(d, 2))
                    if on(0):
                        pe.wait_ge(v_out, upto(a, 2))
                    elif on(-0) or i < NG + 1:
                        pe.wait_ge(relu_done, upto(i - 2, 8))
                    for fi in range(CH):
                        mm = pe.matmul(bank[3][:, :], w_u1[:, fi, :], n4T[:, fi, :],
                                       start=(fi == 0), stop=(fi == CH - 1))
                    mm.then_inc(u1_mm, 1)

                    def up(j):
                        r = RANK * (j % 2)
                        if j < 4:
                            if j == 0:
                                pe.wait_ge(pT_done, upto(d, 1))
                            if j == 2 and on(0):
                                pe.wait_ge(r_gate, upto(a, 2))
                        else:
                            pe.wait_ge(gelu_done, upto(d, 8, j - 3))
                        pe.matmul(bank[HIDDEN_BANKS[j % 4]][:, :], w_v1[r:r + RANK, j // 2, :],
                                  pT[r:r + RANK, :], start=True, stop=True).then_inc(v1_mm, 1)

                    def down(j):
                        r = RANK * (j % 2)
                        pe.wait_ge(gelu_done, upto(d, 8, j + 1))
                        mm = pe.matmul(bank[4][r:r + RANK, :], w_u2[:, j, :], hidden[:, j, :],
                                       start=(j < 2), stop=(j >= FT - 2))
                        if j == FT - 1:
                            mm.then_inc(u2_mm, 1)

                    for j in range(0, FT, 2):
                        up(j)
                        up(j + 1)
                        if j >= 2:
                            down(j - 2)
                            down(j - 1)
                    down(FT - 2)
                    down(FT - 1)
                    pe.wait_ge(gelu_done, upto(d, 8))
                    pe.wait_ge(qT_done, upto(d, 1))
                    for s in range(2):
                        for t in (2 * s, 2 * s + 1):
                            mm = pe.matmul(bank[s][:, C * (t % 2):C * (t % 2) + C], qT[:, P * t:P * t + P],
                                           w_v2[:, :], start=True, stop=True)
                        mm.then_inc(v2_mm, 1)
                if on(1):
                    pe.wait_ge(xr2_done, upto(b, 1))
                    if on(3):
                        pe.wait_ge(qT_done, upto(d, 1))
                    elif some(b):
                        pe.wait_ge(rec_gate, upto(b - 1, 2))
                    token_major((4, 5), xr, w_rec, rec_mm)
                    pe.wait_ge(xk2_done, upto(b, 1))
                    for j in range(FT):
                        if j == 0:
                            if on(0):
                                pe.wait_ge(v_out, upto(a, 2))
                            elif some(b):
                                pe.wait_ge(relu_done, upto(b - 1, 8))
                        if j == 2:
                            if on(3):
                                pe.wait_ge(y_done, upto(d, 2))
                            if on(0):
                                pe.wait_ge(r_gate, upto(a, 2))
                        if j >= 4:
                            pe.wait_ge(relu_done, upto(b, 8, j - 3))
                        for fi in range(CH):
                            mm = pe.matmul(bank[HIDDEN_BANKS[j % 4]][:, :], w_key[:, fi, P * j:P * j + P],
                                           xk[:, fi, :], start=(fi == 0), stop=(fi == CH - 1))
                        mm.then_inc(key_mm, 1)
                for s in range(2):
                    if on(1):
                        if s == 0:
                            pe.wait_ge(h2_done, upto(b, 2))
                        for t in (2 * s, 2 * s + 1):
                            for j in range(FT):
                                if t == 0:
                                    pe.wait_ge(square_done, upto(b, 8, j + 1))
                                mm = pe.matmul(bank[6 + s][:, C * (t % 2):C * (t % 2) + C],
                                               hidden[:, j, P * t:P * t + P], w_val[:, j, :],
                                               start=(j == 0), stop=(j == FT - 1))
                        mm.then_inc(val_mm, 1)
                    if s == 0 and on(-1):
                        pe.wait_ge(n1_done, upto(a + 1, 1))
                        if on(1):
                            pe.wait_ge(relu_done, upto(b, 8))
                        elif on(0):
                            pe.wait_ge(v_out, upto(a, 2))
                        transposes((2, 3), n1[(p + 1) % 2], tr1_mm)

            drive(pe, step)

        @block.vector
        def _(dve):
            dve.wait_ge(decay_exp, 1)
            dve.tensor_scalar(decay[:, :], decay[:, :], -1.0, None, ALU.mult).then_inc(decay_done, 1)
            dve.memset(decay_row[:, :, :], 1.0).then_inc(decay_done, 1)
            dve.wait_ge(decay_done, 2)
            for f in range(CH):
                dve.tensor_scalar(decay_row[:, f, :], decay_row[:, f, :], decay[:, f:f + 1], None, ALU.mult)\
                    .then_inc(decay_done, 1)
            dve.wait_ge(decay_done, 4)
            dve.wait_ge(const_done, 1)
            dve.wait_ge(vec_loaded, 16)

            def norm_stats(n, g, src, tiles, last=True):
                for t in tiles:
                    ins = dve.bn_stats(stat[n][:, t, :], src[:, t, :])
                if last:
                    ins.then_inc(stats_read[n], 1)

            def norm_mean(n, g):
                dve.wait_ge(stats_read[n], upto(g, 1))
                dve.memset(waited[:, :], 0.0)
                for t in range(TT):
                    ins = dve.bn_aggr(mv[n][:, t, :], stat[n][:, t, :])
                ins.then_inc(mean_var[n], 1)

            def normalise(n, g, dst, src, done):
                dve.wait_ge(rstd_done[n], upto(g, 1))
                for t in range(TT):
                    ins = dve.tensor_scalar(dst[:, t, :], src[:, t, :], mv[n][:, t, 0:1], rstd[n][:, t:t + 1],
                                            ALU.subtract, ALU.mult)
                ins.then_inc(done, 1)

            def shift_diff(h, done):
                dve.tensor_tensor(diff[:, :, :].rearrange("p f (s t) -> p (f s) t", s=SEQ),
                                  h[:, :, 1:T + 1], h[:, :, 0:T], ALU.subtract).then_inc(done, 1)

            def mix(dst, h, name, done):
                for f in range(CH):
                    ins = dve.scalar_tensor_tensor(out=seqs(dst, f), in0=seqs(diff, f), scalar=col(name, f),
                                                   in1=before(h, f), op0=ALU.mult, op1=ALU.add)
                ins.then_inc(done, 1)

            def step(i, p, on):
                a, b, c, d = i, i - 1, i - 2, i - 3

                def diagonal_rows(rows, n):
                    first = rows[:, n, 0:n + 1].unsqueeze(1).to_broadcast([P, NB, n + 1])
                    ap = [list(v) for v in first.ap]
                    ap[1][0] = HB * NH + HB
                    return bass.AP(first.tensor, first.offset, ap)

                def sum_scores(t, slot):
                    dve.wait_ge(s_prod, upto(c, 4, t + 1))
                    rows = score[:, NH * t:NH * t + NH, :]
                    for kind, n, at in S_PARTS:
                        if kind == "rect":
                            o = rows[:, HB * n:HB * n + HB, 0:HB * n]
                            m, k = HB, HB * n
                        else:
                            o = diagonal_rows(rows, n)
                            m, k = NB, n + 1
                        src = prod[slot][:, at:at + m * k * HD].rearrange("p (a b d) -> p a b d", a=m, b=k)
                        ins = dve.tensor_reduce(o, src, AX.X, ALU.add)
                    ins.then_inc(s_sum, 1)

                def shift_scores(s):
                    rows = slice(2 * NH * s, 2 * NH * s + 2 * NH)
                    dve.wait_ge(s_sum, upto(c, 4, 2 * s + 2))
                    dve.tensor_reduce(top[:, rows], score[:, rows, :], AX.X, ALU.max).then_inc(top_done, 1)
                    dve.wait_ge(top_done, upto(c, 2, s + 1))
                    if some(c):
                        dve.wait_ge(v_prod, upto(c - 1, 4))
                    dve.tensor_tensor(prob[:, rows, :], score[:, rows, :],
                                      top[:, rows].unsqueeze(2).to_broadcast([P, 2 * NH, NH]), ALU.subtract)\
                        .then_inc(shift_done, 1)

                def inverse_mass(s):
                    rows = slice(2 * NH * s, 2 * NH * s + 2 * NH)
                    dve.wait_ge(prob_done, upto(c, 2, s + 1))
                    dve.tensor_reduce(mass[:, rows], prob[:, rows, :], AX.X, ALU.add).then_inc(mass_done, 1)
                    dve.wait_ge(mass_done, upto(c, 2, s + 1))
                    dve.reciprocal(mass[:, rows], mass[:, rows]).then_inc(inv_done, 1)

                def sum_values(g, t, slot):
                    dve.wait_ge(v_prod, upto(g, 4, t + 1))
                    for n, keys, at in V_PARTS:
                        src = prod[slot][:, at:at + HB * HD * keys].rearrange("p (a b) -> p a b", b=keys)
                        o = o_att[:, NH * t + HB * n:NH * t + HB * n + HB, :].rearrange("p h d -> p (h d)")
                        ins = dve.tensor_reduce(o, src, AX.X, ALU.add)
                    ins.then_inc(v_sum, 1)

                def attention_residual(g, par, s):
                    rows = slice(2 * NH * s, 2 * NH * s + 2 * NH)
                    dve.wait_ge(v_sum, upto(g, 4, 2 * s + 2))
                    dve.wait_ge(inv_done, upto(g, 2, s + 1))
                    dve.tensor_tensor(o_att[:, rows, :], o_att[:, rows, :],
                                      mass[:, rows].unsqueeze(2).to_broadcast([P, 2 * NH, HD]), ALU.mult)\
                        .then_inc(o_norm, 1)
                    dve.wait_ge(o_norm, upto(g, 2, s + 1))
                    if s == 0 and some(g):
                        dve.wait_ge(x3b_done, upto(g - 1, 1))
                    dve.tensor_tensor(pair(x3, s), o_att[:, rows, :].rearrange("p h d -> p (h d)"),
                                      pair(x2[par], s), ALU.add).then_inc(x3_done, 1)

                if on(2):
                    for s in range(2):
                        dve.wait_ge(val_mm, upto(c, 2, s + 1))
                        dve.wait_ge(rec_gate, upto(c, 2, s + 1))
                        dve.scalar_tensor_tensor(out=pair(gate_rec, s), in0=pair(gate_rec, s), scalar=1.0,
                                                 in1=bank[6 + s][:, :], op0=ALU.add, op1=ALU.mult)\
                            .then_inc(gated_done, 1)
                    dve.wait_ge(res_done, upto(c, 1))
                    for s in range(2):
                        dve.wait_ge(gated_done, upto(c, 2, s + 1))
                        dve.scalar_tensor_tensor(out=pair(x2[p], s), in0=pair(gate_rec, s), scalar=0.5,
                                                 in1=pair(x1, s), op0=ALU.mult, op1=ALU.add)\
                            .then_inc(x2_done, 1)
                    dve.wait_ge(x2_done, upto(c, 2))
                    norm_stats(3, c, x2[p], range(TT))
                    norm_mean(3, c)
                if on(0):
                    for f in range(CH):
                        dve.wait_ge(k_out, upto(a, 2, f + 1))
                        for s in range(SEQ):
                            ins = dve.tensor_tensor_scan(pp[:, SEQ * f + s, 1:T + 1], decay_row[:, f, :],
                                                         kT[:, f, T * s:T * s + T], START, ALU.add, ALU.max)
                        ins.then_inc(pp_done, 1)
                if on(2):
                    if some(c):
                        dve.wait_ge(s_prod, upto(c - 1, 4))
                    normalise(3, c, q, x2[p], q_done)
                if on(0):
                    for f in range(CH):
                        dve.wait_ge(pp_done, upto(a, 2, f + 1))
                        dve.scalar_tensor_tensor(out=seqs(e1, f), in0=before(pp, f), scalar=decay[:, f:f + 1],
                                                 in1=now(pp, f), op0=ALU.add, op1=ALU.subtract)\
                            .then_inc(e1_arg, 1)
                    for f in range(CH):
                        if some(a):
                            dve.wait_ge(rwkv_done, upto(a - 1, 2))
                        dve.scalar_tensor_tensor(out=seqs(rr, f), in0=seqs(kT, f), scalar=col("time_first", f),
                                                 in1=before(pp, f), op0=ALU.add, op1=ALU.subtract)\
                            .then_inc(rr_raw, 1)
                if on(1):
                    for s in range(2):
                        dve.wait_ge(wo_mm, upto(b, 2, s + 1))
                        for t in (2 * s, 2 * s + 1):
                            ins = dve.scalar_tensor_tensor(
                                out=x1[:, t, :], in0=n1[(p + 1) % 2][:, t, :], scalar=back[(p + 1) % 2][:, t:t + 1],
                                in1=bank[6 + s][:, C * (t % 2):C * (t % 2) + C], op0=ALU.mult, op1=ALU.add)
                        ins.then_inc(x1_done, 1)
                    dve.wait_ge(x1_done, upto(b, 2))
                    norm_stats(2, b, x1, range(TT))
                    norm_mean(2, b)
                if on(0):
                    for f in range(CH):
                        dve.wait_ge(rr_raw, upto(a, 2, f + 1))
                        dve.tensor_scalar(rr[:, f, :], rr[:, f, :], GAP, None, ALU.min).then_inc(rr_arg, 1)
                if on(3):
                    sum_values(d, 3, 0)
                if on(1):
                    if some(b):
                        dve.wait_ge(tr2_mm, upto(b - 1, 2))
                    normalise(2, b, n2, x1, n2_done)
                if on(3):
                    attention_residual(d, (p + 1) % 2, 1)
                    dve.wait_ge(x3_done, upto(d, 2))
                    norm_stats(4, d, x3, (2, 3))
                    norm_mean(4, d)
                if on(2):
                    sum_scores(0, 1)
                if on(3):
                    if some(d):
                        dve.wait_ge(tr4_mm, upto(d - 1, 2))
                    normalise(4, d, n4, x3, n4_done)
                if on(0):
                    for f in range(CH):
                        dve.wait_ge(e1_exp, upto(a, 2, f + 1))
                        dve.wait_ge(e2_exp, upto(a, 2, f + 1))
                        if some(a):
                            dve.wait_ge(den_done, upto(a - 1, 2))
                        for s in range(SEQ):
                            cols = slice(T * s, T * s + T)
                            ins = dve.tensor_tensor_scan(bb[:, SEQ * f + s, 1:T + 1], e1[:, f, cols],
                                                         e2[:, f, cols], 0.0, ALU.mult, ALU.add)
                        ins.then_inc(bb_done, 1)
                        dve.wait_ge(e2v_done, upto(a, 2, f + 1))
                        if some(a):
                            dve.wait_ge(num_done, upto(a - 1, 2))
                        for s in range(SEQ):
                            cols = slice(T * s, T * s + T)
                            ins = dve.tensor_tensor_scan(aa[:, SEQ * f + s, 1:T + 1], e1[:, f, cols],
                                                         num[:, f, cols], 0.0, ALU.mult, ALU.add)
                        ins.then_inc(aa_done, 1)
                if on(2):
                    sum_scores(1, 0)
                if on(1):
                    dve.wait_ge(h2_done, upto(b, 2))
                    shift_diff(h, diff2_done)
                    dve.wait_ge(diff2_done, upto(b, 1))
                    if some(b):
                        dve.wait_ge(rec_mm, upto(b - 1, 2))
                    if on(0):
                        dve.wait_ge(r_mm, upto(a, 2))
                    mix(xr, h, "ffn_tmr", xr2_done)
                    if some(b):
                        dve.wait_ge(key_mm, upto(b - 1, 8))
                    if on(0):
                        dve.wait_ge(k_mm, upto(a, 2))
                    mix(xk, h, "ffn_tmk", xk2_done)
                    dve.wait_ge(x_again, 16 * (b + 1))
                    dve.tensor_tensor(x1[:, :, :], x1[:, :, :], n1[(p + 1) % 2][:, :, :], ALU.add)\
                        .then_inc(res_done, 1)
                if on(2):
                    shift_scores(0)
                    sum_scores(2, 1)
                if on(3):
                    dve.wait_ge(x3b_done, upto(d, 1))
                    for s in range(2):
                        dve.wait_ge(v2_mm, upto(d, 2, s + 1))
                        dve.tensor_tensor(pair(y_out, s), bank[s][:, :], pair(y_out, s), ALU.add)\
                            .then_inc(y_done, 1)
                if on(2):
                    sum_scores(3, 0)
                    inverse_mass(0)
                    shift_scores(1)
                if on(-1):
                    g = a + 1
                    dve.wait_ge(x_loaded, 16 * (g + 1))
                    norm_stats(1, g, x_in, range(TT))
                    norm_mean(1, g)
                    dve.wait_ge(inv1_done, upto(g, 1))
                    dve.tensor_tensor(vx[:, :], mv[1][:, :, 1], inv1[:, :], ALU.mult).then_inc(vx_done, 1)
                if on(2):
                    sum_values(c, 0, 1)
                if on(-1):
                    dve.wait_ge(lnx_done, upto(g, 1))
                    dve.tensor_tensor(lnv[1][:, :], lnv[1][:, :], lnx[:, :], ALU.add).then_inc(lnsum_done, 1)
                    if some(g - 1):
                        dve.wait_ge(tr1_mm, upto(g - 2, 2))
                    normalise(1, g, n1[(p + 1) % 2], x_in, n1_done)
                if on(2):
                    sum_values(c, 1, 0)
                    attention_residual(c, p, 0)
                    inverse_mass(1)
                    dve.wait_ge(x3_done, upto(c, 2, 1))
                    norm_stats(4, c, x3, (0, 1), last=False)
                if on(0):
                    for f in range(CH):
                        dve.wait_ge(r_gate, upto(a, 2, f + 1))
                        dve.wait_ge(num_done, upto(a, 2, f + 1))
                        dve.scalar_tensor_tensor(out=num[:, f, :], in0=gate_r[:, f, :], scalar=1.0,
                                                 in1=num[:, f, :], op0=ALU.add, op1=ALU.mult)\
                            .then_inc(gnum_done, 1)
                    for f in range(CH):
                        dve.wait_ge(gnum_done, upto(a, 2, f + 1))
                        dve.wait_ge(den_inv, upto(a, 2, f + 1))
                        dve.tensor_tensor(num[:, f, :], num[:, f, :], rr[:, f, :], ALU.mult)\
                            .then_inc(rwkv_done, 1)
                if on(-1):
                    dve.wait_ge(h1_done, upto(g, 2))
                    shift_diff(h, diff1_done)
                    dve.wait_ge(diff1_done, upto(g, 1))
                    if some(g):
                        dve.wait_ge(k_mm, upto(g - 1, 2))
                    if on(1):
                        dve.wait_ge(key_mm, upto(b, 8))
                    mix(xk, h, "att_tmk", xk_done)
                    if some(g):
                        dve.wait_ge(v_mm, upto(g - 1, 2))
                    mix(xv, h, "att_tmv", xv_done)
                    if some(g):
                        dve.wait_ge(r_mm, upto(g - 1, 2))
                    if on(1):
                        dve.wait_ge(rec_mm, upto(b, 2))
                    mix(xr, h, "att_tmr", xr_done)
                if on(2):
                    sum_values(c, 2, 1)

            drive(dve, step)


def kernel(**inputs):
    import numpy as _np
    import concourse.bacc as _bacc
    from concourse import mybir as _mybir
    from concourse.bass_utils import run_bass_kernel_spmd as _run

    def att(name):
        return _np.asarray(inputs["L0_attn_" + name])

    def ffn(name):
        return _np.asarray(inputs["L0_ffn_" + name])

    columns = [att(n).reshape(CH, P).T for n in VECS] + [ffn("b1").reshape(FT, P).T]
    data = {
        "x": inputs["x"], "ctx": inputs["ctx_1024"], "vecs": _np.concatenate(columns, axis=1),
        "b2": ffn("b2").reshape(1, C), "wk": att("Wk").T, "wv": att("Wv").T, "wr": att("Wr").T,
        "wo": att("Wo").T, "wkey": att("Wkey").T, "wrec": att("Wrec").T, "wval": att("Wval").T,
        "u1": ffn("U1"), "v1": ffn("V1"), "u2": ffn("U2"), "v2": ffn("V2"),
    }
    nc = _bacc.Bacc("TRN2", target_bir_lowering=False, num_devices=1)
    arrays, args = {}, []
    for name, a in data.items():
        a = _np.ascontiguousarray(a)
        arrays[f"in_{name}"] = a
        args.append(nc.dram_tensor(f"in_{name}", a.shape, _mybir.dt.from_np(a.dtype), kind="ExternalInput").ap())
    args.append(nc.dram_tensor("out_0", arrays["in_x"].shape, _mybir.dt.float32, kind="ExternalOutput").ap())
    build(nc, *args)
    r = _run(nc, [arrays], core_ids=[0])
    return r.results[0]["out_0"]
```
